# Optimizing a Trainium2 kernel written in Bass

```python
import numpy as np
import jax
import jax.numpy as jnp

def _softmax(x, axis=-1):
    return jax.nn.softmax(x, axis=axis)

def _gelu(x):
    return jax.nn.gelu(x, approximate=True)

def _silu(x):
    return jax.nn.silu(x)

def _sigmoid(x):
    return jax.nn.sigmoid(x)

def _layernorm(x, axis=-1, eps=1e-05):
    m = jnp.mean(x, axis=axis, keepdims=True)
    v = jnp.var(x, axis=axis, keepdims=True)
    return (x - m) / jnp.sqrt(v + eps)

def _scatter_add(tgt, idx, src, axis=0):
    return tgt.at[idx].add(src)

def _segment_sum(src, seg, n):
    return jax.ops.segment_sum(src, seg, n)
kernel_name = 'mk_gnn_preln_d1_gnn_r32_d316df'

def setup_inputs(seed: int=0):
    np.random.seed(seed)
    _w = jnp.asarray

    def _rec_inputs():
        import jax
        import jax.numpy as jnp
        _gk = jax.random.key(seed)
        x = -0.0009044 + 1 * jax.random.normal(jax.random.fold_in(_gk, 1), (3125, 16), jnp.float32)
        src = jax.random.randint(jax.random.fold_in(_gk, 2), (100000,), 0, 3125, jnp.int32)
        dst = jnp.minimum((3125 * jax.random.uniform(jax.random.fold_in(_gk, 3), (100000,)) ** 2.0).astype(jnp.int32), 99999)
        _o = jnp.argsort(dst, stable=True)
        src = src[_o]
        dst = dst[_o]
        edge_attr_8 = 0.000398945 + 1.00003 * jax.random.normal(jax.random.fold_in(_gk, 11), (100000, 8), jnp.float32)
        return (x, src, dst, edge_attr_8)
    x, src, dst, edge_attr_8 = _rec_inputs()

    def _L0_gnn_setup():
        import jax, jax.numpy as jnp
        import numpy as np
        N_NODES = 3125
        N_EDGES = 25000
        IN_C = 16
        OUT_C = 16
        EDGE_DIM = 8
        HIDDEN = 64

        def _layernorm(h, w, b, eps=1e-05):
            mu = jnp.mean(h, axis=-1, keepdims=True)
            var = jnp.mean(jnp.square(h - mu), axis=-1, keepdims=True)
            return (h - mu) * jax.lax.rsqrt(var + eps) * w + b
        key = jax.random.key(seed)
        ks = jax.random.split(key, 12)
        x = jax.random.normal(ks[0], (N_NODES, IN_C), dtype=jnp.float32)
        edge_index = jax.random.randint(ks[1], (2, N_EDGES), 0, N_NODES, dtype=jnp.int64)
        edge_attr = jax.random.normal(ks[2], (N_EDGES, EDGE_DIM), dtype=jnp.float32)
        s1 = 1.0 / np.sqrt(EDGE_DIM)
        s2 = 1.0 / np.sqrt(HIDDEN)
        s3 = 1.0 / np.sqrt(IN_C)
        W1 = jax.random.uniform(ks[3], (EDGE_DIM, HIDDEN), jnp.float32, -s1, s1)
        b1 = jax.random.uniform(ks[4], (HIDDEN,), jnp.float32, -s1, s1)
        W2 = jax.random.uniform(ks[5], (HIDDEN, OUT_C * IN_C), jnp.float32, -s2, s2)
        b2 = jax.random.uniform(ks[6], (OUT_C * IN_C,), jnp.float32, -s2, s2)
        root = jax.random.uniform(ks[7], (IN_C, OUT_C), jnp.float32, -s3, s3)
        bias = jnp.zeros((OUT_C,), jnp.float32)
        ln_w = jnp.ones((OUT_C,), jnp.float32)
        ln_b = jnp.zeros((OUT_C,), jnp.float32)
        return {'x': x, 'edge_index': edge_index, 'edge_attr': edge_attr, 'W1': W1, 'b1': b1, 'W2': W2, 'b2': b2, 'root': root, 'bias': bias, 'ln_w': ln_w, 'ln_b': ln_b}
    _L0_gnn_all = _L0_gnn_setup()
    _L0_gnn_in = {k: v for k, v in _L0_gnn_all.items() if k in ('W1', 'b1', 'W2', 'b2', 'root', 'bias', 'ln_w', 'ln_b')}
    del _L0_gnn_all
    return {'x': x, 'src': src, 'dst': dst, 'edge_attr_8': edge_attr_8, 'L0_gnn_W1': _L0_gnn_in['W1'], 'L0_gnn_b1': _L0_gnn_in['b1'], 'L0_gnn_W2': _L0_gnn_in['W2'], 'L0_gnn_b2': _L0_gnn_in['b2'], 'L0_gnn_root': _L0_gnn_in['root'], 'L0_gnn_bias': _L0_gnn_in['bias'], 'L0_gnn_ln_w': _L0_gnn_in['ln_w'], 'L0_gnn_ln_b': _L0_gnn_in['ln_b']}

def reference(x, src, dst, edge_attr_8, L0_gnn_W1, L0_gnn_b1, L0_gnn_W2, L0_gnn_b2, L0_gnn_root, L0_gnn_bias, L0_gnn_ln_w, L0_gnn_ln_b):
    import jax
    import jax.numpy as jnp

    def _L0_gnn_ref(x, edge_index, edge_attr, W1, b1, W2, b2, root, bias, ln_w, ln_b):
        import jax, jax.numpy as jnp
        import numpy as np
        N_NODES = 3125
        N_EDGES = 25000
        IN_C = 16
        OUT_C = 16
        EDGE_DIM = 8
        HIDDEN = 64

        def _layernorm(h, w, b, eps=1e-05):
            mu = jnp.mean(h, axis=-1, keepdims=True)
            var = jnp.mean(jnp.square(h - mu), axis=-1, keepdims=True)
            return (h - mu) * jax.lax.rsqrt(var + eps) * w + b
        src = edge_index[0]
        dst = edge_index[1]
        h = jax.nn.silu(edge_attr @ W1 + b1)
        We = (h @ W2 + b2).reshape(-1, IN_C, OUT_C)
        msg = jnp.einsum('ei,eio->eo', x[src], We)
        summed = jax.ops.segment_sum(msg, dst, num_segments=N_NODES)
        cnt = jax.ops.segment_sum(jnp.ones_like(dst, dtype=x.dtype), dst, num_segments=N_NODES)
        aggr = summed / jnp.maximum(cnt, 1.0)[:, None]
        out = aggr + x @ root + bias
        out = _layernorm(out, ln_w, ln_b)
        return jax.nn.silu(out + x)
    edge_index = jnp.stack([src, dst])
    h = jnp.maximum(_layernorm(x, axis=-1), 0.0)
    x = x + _L0_gnn_ref(h, edge_index, edge_attr_8, L0_gnn_W1, L0_gnn_b1, L0_gnn_W2, L0_gnn_b2, L0_gnn_root, L0_gnn_bias, L0_gnn_ln_w, L0_gnn_ln_b)
    return x

_drawn_inputs = setup_inputs


def setup_inputs(seed=0):
    import zlib

    import numpy as np

    out = dict(_drawn_inputs(seed))
    spreads = {'L0_gnn_bias': (0.0, 0.1), 'L0_gnn_ln_w': (1.0, 0.2), 'L0_gnn_ln_b': (0.0, 0.1)}
    factors = {}
    for name, (base, spread) in spreads.items():
        noise = np.random.default_rng([zlib.crc32(name.encode()), seed]).standard_normal(out[name].shape)
        drawn = base * np.exp(spread * noise) if base else spread * noise
        out[name] = jnp.asarray(drawn.astype(out[name].dtype))
    for name, factor in factors.items():
        out[name] = (out[name] * factor).astype(out[name].dtype)
    return out
```

```python
import concourse.bass as bass
from concourse import mybir
from contextlib import ExitStack

P = 128
N_NODES = 3125
N_EDGES = 100000
C = 16
ED = 8
HID = 64
TILES = 4
GE = TILES * P
NG = -(-N_EDGES // GE)
WINS = -(-N_NODES // P)
MC = C + 1
PAD_DST = WINS * P
BUFS = 4
EPS = 1e-5


def gnn_layer(nc, x, edge_t, edge_ix, dst_rows, w1, b1, w2e, root, rows, x_table, span_table, out):
    fp32, i32 = mybir.dt.float32, mybir.dt.int32
    ALU, ACT, AX = mybir.AluOpType, mybir.ActivationFunctionType, mybir.AxisListType
    ROWS2 = NG // 2
    FULL = N_NODES // P
    REST = N_NODES - FULL * P
    KC = P // C
    CH = -(-WINS // KC)

    with ExitStack() as ctx:
        def sb(name, shape, dt=fp32):
            return ctx.enter_context(nc.sbuf_tensor(name, shape, dt))

        def ps(name, shape):
            return ctx.enter_context(nc.psum_tensor(name, shape, fp32))

        def sem(name):
            return ctx.enter_context(nc.semaphore(name))

        x_in = sb("x_in", [P, WINS, C])
        xh = sb("xh", [P, WINS, C])
        sq = sb("sq", [P, WINS, C])
        cen = sb("cen", [P, WINS, C])
        root_part = sb("root_part", [P, WINS, C])
        stat = sb("stat", [P, 4, WINS])
        row_params = sb("row_params", [P, 3, C])
        ident = sb("ident", [P, P])
        root_diag = sb("root_diag", [P, P])
        xT = sb("xT", [P, CH, P])
        node_i = sb("node_i", [P, WINS * P], i32)
        node_f = sb("node_f", [P, WINS * P])
        dst_sb = sb("dst_sb", [ROWS2, 2, GE], i32)
        span_f = sb("span_f", [ROWS2, 2, 2], i32)
        span_w = sb("span_w", [ROWS2, 2, 2], i32)
        spans = sb("spans", [1, NG * 2], i32)
        w1_sb = sb("w1_sb", [ED, HID])
        b1_sb = sb("b1_sb", [HID, 1])
        w2_sb = sb("w2_sb", [HID + 1, C * C])
        ea = [sb(f"ea{i}", [ED, GE]) for i in range(BUFS)]
        ix = [sb(f"ix{i}", [P, 2 * TILES], i32) for i in range(BUFS)]
        xg = [sb(f"xg{i}", [P, TILES, C]) for i in range(BUFS)]
        hT = [sb(f"hT{i}", [HID + 1, GE]) for i in range(2)]
        prod = [sb(f"prod{i}", [P, TILES, C, C]) for i in range(2)]
        msg = [sb(f"msg{i}", [P, TILES, MC]) for i in range(2)]
        onehot = sb("onehot", [P, TILES, P])

        acc = ps("acc", [P, 512])
        hps = [ps(f"hps{i}", [P, 512]) for i in range(2)]
        we = [ps(f"we{i}", [P, TILES, C * C]) for i in range(2)]
        pT = ps("pT", [P, 512])

        s_x = sem("s_x")
        s_par = sem("s_par")
        s_w = sem("s_w")
        s_dst = sem("s_dst")
        s_ones = sem("s_ones")
        s_iota = sem("s_iota")
        s_id0 = sem("s_id0")
        s_id = sem("s_id")
        s_dz = sem("s_dz")
        s_diag = sem("s_diag")
        s_v = sem("s_v")
        s_var = sem("s_var")
        s_sd = sem("s_sd")
        s_xh = sem("s_xh")
        s_table = sem("s_table")
        s_xT = sem("s_xT")
        s_xTc = sem("s_xTc")
        s_root = sem("s_root")
        s_spanw = sem("s_spanw")
        s_spand = sem("s_spand")
        s_span = sem("s_span")
        s_ea = [sem(f"s_ea{i}") for i in range(BUFS)]
        s_ix = [sem(f"s_ix{i}") for i in range(BUFS)]
        s_gath = [sem(f"s_gath{i}") for i in range(BUFS)]
        s_hps = sem("s_hps")
        s_h = sem("s_h")
        s_we = sem("s_we")
        s_prod = sem("s_prod")
        s_msg = sem("s_msg")
        s_oh = sem("s_oh")
        s_scat = sem("s_scat")
        s_pre = sem("s_pre")
        s_act = sem("s_act")
        s_fin = sem("s_fin")
        s_out = sem("s_out")

        block = ctx.enter_context(nc.Block())

        def buf(n):
            return n % BUFS

        def rounds(n, b):
            return (n - b) // BUFS + 1

        def loop_groups(eng, step):
            for b in range(BUFS):
                step(b, b, b, False, 1)
            with eng.Fori(1, NG // BUFS - 1) as it:
                for b in range(BUFS):
                    step(it * BUFS + b, b, None, False, it + 1)
            for b in range(BUFS):
                step(NG - BUFS + b, b, None, b == BUFS - 1, NG // BUFS)

        @block.sync
        def _(sp):
            sp.dma_start(x_in[:, :, :], x.rearrange("(w p) c -> p w c", p=P)).then_inc(s_x, 16)
            sp.dma_start(row_params[:, :, :], rows).then_inc(s_par, 16)
            sp.dma_start(dst_sb[:, :, :], dst_rows.rearrange("(r h) e -> r h e", h=2)).then_inc(s_dst, 16)

            def load(n, b, early, last, k):
                if early is None:
                    sp.wait_ge(s_hps, n - BUFS + 1)
                sp.dma_start(ea[b][:, :], edge_t[bass.ds(n, 1), :, :].rearrange("a f e -> (a f) e")).then_inc(s_ea[b], 16)
                if early is None:
                    sp.wait_ge(s_prod, n - BUFS + 2)
                sp.dma_start(ix[b][:, :], edge_ix[bass.ds(n, 1), :, :].rearrange("a p t -> (a p) t")).then_inc(s_ix[b], 16)

            for b in range(BUFS):
                load(b, b, b, False, 1)
            sp.wait_ge(s_xh, 1)
            sp.dma_start(x_table.rearrange("(w p) c -> p w c", p=P), xh[:, :, :]).then_inc(s_table, 16)
            sp.wait_ge(s_spanw, 1)
            sp.dma_start(span_table.rearrange("(r k) -> r k", k=4), span_w[:, :, :].rearrange("r a b -> r (a b)")).then_inc(s_spand, 16)
            sp.wait_ge(s_spand, 16)
            sp.dma_start(spans[:, :], span_table.rearrange("(a k) -> a k", a=1)).then_inc(s_span, 16)
            with sp.Fori(1, NG // BUFS - 1) as it:
                for b in range(BUFS):
                    load(it * BUFS + b, b, None, False, it + 1)
            for b in range(BUFS):
                load(NG - BUFS + b, b, None, False, NG // BUFS)
            sp.wait_ge(s_table, 16)
            sp.wait_ge(s_fin, 1)
            sp.dma_start(out[0:FULL * P, :].rearrange("(w p) c -> p w c", p=P), cen[:, 0:FULL, :]).then_inc(s_out, 16)
            sp.dma_start(out[FULL * P:N_NODES, :], cen[0:REST, FULL, :]).then_inc(s_out, 16)
            sp.wait_ge(s_out, 32)

        @block.gpsimd
        def _(pool):
            nc.gpsimd.memset(ident[:, :], 0.0).then_inc(s_id0, 1)
            nc.gpsimd.memset(root_diag[:, :], 0.0).then_inc(s_dz, 1)
            pool.wait_ge(s_id0, 1)
            nc.gpsimd.affine_select(out=ident[:, :], in_=ident[:, :], compare_op=ALU.not_equal, fill=1.0,
                                    base=0, pattern=[[-1, P]], channel_multiplier=1).then_inc(s_id, 1)
            nc.gpsimd.iota(node_i[:, :], pattern=[[1, WINS * P]], base=0, channel_multiplier=0).then_inc(s_iota, 1)
            pool.wait_ge(s_table, 16)

            multiplied = pool.alloc_register("groups_multiplied")
            pool.reg_mov(multiplied, 1)

            def gather(n, b, early, last, k):
                if early is None and not isinstance(n, int):
                    so_far = pool.snap(multiplied, min_val=1, max_val=NG)
                    filled = pool.snap(16 * k)
                    pool.wait_ge(s_ix[b], filled)
                    pool.wait_ge(s_prod, so_far)
                    pool.reg_add(multiplied, multiplied, 1)
                else:
                    pool.wait_ge(s_ix[b], 16 * k)
                    if early is None:
                        pool.wait_ge(s_prod, n - BUFS + 1)
                for t in range(TILES):
                    pool.indirect_dma_start(
                        out=xg[b][:, t, :], out_offset=None, in_=x_table,
                        in_offset=bass.IndirectOffsetOnAxis(ap=ix[b][:, t:t + 1], axis=0)).then_inc(s_gath[b], 16)

            loop_groups(pool, gather)

        @block.scalar
        def _(act):
            act.dma_start(w1_sb[:, :], w1).then_inc(s_w, 16)
            act.dma_start(b1_sb[:, :], b1).then_inc(s_w, 16)
            act.dma_start(w2_sb[:, :], w2e).then_inc(s_w, 16)
            act.wait_ge(s_dz, 1)
            for k in range(KC):
                act.dma_start(root_diag[k * C:(k + 1) * C, k * C:(k + 1) * C], root).then_inc(s_diag, 16)
            act.wait_ge(s_var, 1)
            nc.scalar.activation(stat[:, 2, :], stat[:, 1, :], ACT.Sqrt).then_inc(s_sd, 1)
            act.wait_ge(s_w, 48)

            def silu(n, b, early, last, k):
                act.wait_ge(s_hps, n + 1)
                if early is None or early >= 2:
                    act.wait_ge(s_we, n - 1)
                nc.scalar.activation(hT[b % 2][0:HID, :], hps[b % 2][0:HID, :], ACT.Silu,
                                     bias=b1_sb[:, 0:1]).then_inc(s_h, 1)

            loop_groups(act, silu)
            act.wait_ge(s_var, 2)
            nc.scalar.activation(stat[:, 2, :], stat[:, 1, :], ACT.Sqrt).then_inc(s_sd, 1)
            act.wait_ge(s_pre, 1)
            nc.scalar.activation(sq[:, :, :], cen[:, :, :], ACT.Silu).then_inc(s_act, 1)

        @block.tensor
        def _(pe):
            pe.wait_ge(s_xh, 1)
            pe.wait_ge(s_id, 1)
            xh_flat = xh[:, :, :].rearrange("p w c -> p (w c)")
            for k in range(CH):
                cols = min(P, WINS * C - k * P)
                last = nc.tensor.transpose(pT[0:cols, k * P:(k + 1) * P], xh_flat[:, k * P:k * P + cols], ident[:, :])
            last.then_inc(s_xT, 1)
            pe.wait_ge(s_xTc, 1)
            pe.wait_ge(s_diag, 16 * KC)
            for k in range(CH):
                cols = min(P, WINS * C - k * P)
                last = nc.tensor.matmul(pT[:, k * P:k * P + cols], xT[0:cols, k, :], root_diag[0:cols, 0:cols],
                                        start=True, stop=True)
            last.then_inc(s_root, 1)

            def hidden(n, b, early, k):
                pe.wait_ge(s_ea[b], 16 * k)
                if early is None or early >= 2:
                    pe.wait_ge(s_h, n - 1)
                nc.tensor.matmul(hps[b % 2][0:HID, :], w1_sb[:, :], ea[b][:, :], start=True, stop=True).then_inc(s_hps, 1)

            def edge_matrices(n, b, early):
                pe.wait_ge(s_h, n + 1)
                if early is None or early >= 2:
                    pe.wait_ge(s_prod, n - 1)
                for t in range(TILES):
                    last = nc.tensor.matmul(we[b % 2][:, t, :], hT[b % 2][:, t * P:(t + 1) * P], w2_sb[:, :],
                                            start=True, stop=True)
                last.then_inc(s_we, 1)

            def scatter(n, b):
                lo = pe.value_load(spans[0:1, bass.ds(2 * n, 1)], min_val=0, max_val=WINS - 1)
                hi = pe.value_load(spans[0:1, bass.ds(2 * n + 1, 1)], min_val=0, max_val=WINS - 1)
                if isinstance(n, int):
                    pe.wait_ge(s_msg, n + 1)
                else:
                    pe.wait_ge(s_msg, pe.snap(messages, min_val=BUFS, max_val=NG))
                    pe.reg_add(messages, messages, 1)
                with pe.Fori(lo, hi + 1) as w:
                    pe.reg_add(done, done, 1)
                    pe.wait_ge(s_oh, pe.snap(done, min_val=1, max_val=NG * WINS))
                    for t in range(TILES):
                        last = nc.tensor.matmul(acc[:, bass.ds(w * MC, MC)], onehot[:, t, :], msg[b % 2][:, t, :],
                                                start=False, stop=False, skip_group_check=True)
                    last.then_inc(s_scat, 1)

            pe.wait_ge(s_w, 48)
            pe.wait_ge(s_ones, 3)
            pe.wait_ge(s_span, 16)
            done = pe.alloc_register("windows_done")
            pe.reg_mov(done, 0)
            messages = pe.alloc_register("message_groups")
            pe.reg_mov(messages, BUFS)
            hidden(0, 0, 0, 1)

            def step(n, b, early, last, k):
                if not last:
                    nb = (b + 1) % BUFS
                    hidden(n + 1, nb, None if early is None or early == BUFS - 1 else early + 1,
                           k + 1 if nb == 0 else k)
                edge_matrices(n, b, early)
                if early != 0:
                    scatter(n - 1, (b - 1) % BUFS)

            loop_groups(pe, step)
            scatter(NG - 1, BUFS - 1)

        @block.vector
        def _(dve):
            chain = [0]

            def link(ins):
                chain[0] += 1
                ins.then_inc(s_v, 1)
                dve.wait_ge(s_v, chain[0])

            def wide(ap, k=C):
                return ap.rearrange("p (w a) -> p w a", a=1).to_broadcast([P, WINS, k])

            def norm(dst, src, sd_at):
                link(nc.vector.tensor_reduce(stat[:, 0, :], src, axis=AX.X, op=ALU.add))
                link(nc.vector.tensor_scalar(stat[:, 3, :], stat[:, 0, :], 1.0 / C, None, ALU.mult))
                link(nc.vector.tensor_tensor(dst, src, wide(stat[:, 3, :]), ALU.subtract))
                link(nc.vector.tensor_tensor(sq[:, :, :], dst, dst, ALU.mult))
                link(nc.vector.tensor_reduce(stat[:, 0, :], sq[:, :, :], axis=AX.X, op=ALU.add))
                nc.vector.tensor_scalar(stat[:, 1, :], stat[:, 0, :], 1.0 / C, EPS, ALU.mult, ALU.add).then_inc(s_var, 1)
                dve.wait_ge(s_sd, sd_at)
                link(nc.vector.reciprocal(stat[:, 3, :], stat[:, 2, :]))
                link(nc.vector.tensor_tensor(dst, dst, wide(stat[:, 3, :]), ALU.mult))

            dve.wait_ge(s_x, 16)
            norm(cen[:, :, :], x_in[:, :, :], 1)
            nc.vector.tensor_scalar(xh[:, :, :], cen[:, :, :], 0.0, None, ALU.max).then_inc(s_xh, 1)
            dve.wait_ge(s_dst, 16)
            nc.vector.tensor_reduce(span_f[:, :, 0], dst_sb[:, :, :], axis=AX.X, op=ALU.min)
            link(nc.vector.tensor_reduce(span_f[:, :, 1], dst_sb[:, :, :], axis=AX.X, op=ALU.max))
            link(nc.vector.tensor_scalar(span_f[:, :, :], span_f[:, :, :], float(N_NODES - 1), None, ALU.min))
            nc.vector.tensor_scalar(span_w[:, :, :], span_f[:, :, :], 7, None, ALU.arith_shift_right).then_inc(s_spanw, 1)
            nc.vector.memset(acc[:, :], 0.0).then_inc(s_ones, 1)
            for i in range(2):
                nc.vector.memset(msg[i][:, :, C:MC], 1.0)
                nc.vector.memset(hT[i][HID:HID + 1, :], 1.0).then_inc(s_ones, 1)
            dve.wait_ge(s_iota, 1)
            link(nc.vector.tensor_copy(node_f[:, :], node_i[:, :]))
            dve.wait_ge(s_xT, 1)
            full = (WINS * C) // P
            nc.vector.tensor_copy(xT[:, 0:full, :], pT[:, 0:full * P].rearrange("p (k n) -> p k n", n=P))
            rest = WINS * C - full * P
            nc.vector.tensor_copy(xT[0:rest, full, :], pT[0:rest, full * P:(full + 1) * P]).then_inc(s_xTc, 1)
            dve.wait_ge(s_root, 1)
            dve.wait_ge(s_par, 16)

            def param(k):
                return row_params[:, k:k + 1, :].to_broadcast([P, WINS, C])

            link(nc.vector.tensor_tensor(root_part[:, :, :], pT[:, 0:WINS * C].rearrange("p (w c) -> p w c", c=C),
                                         param(0), ALU.add))
            dve.wait_ge(s_span, 16)
            made = dve.alloc_register("windows_made")
            dve.reg_mov(made, 0)

            def step(n, b, early, last, k):
                lo = dve.value_load(spans[0:1, bass.ds(2 * n, 1)], min_val=0, max_val=WINS - 1)
                hi = dve.value_load(spans[0:1, bass.ds(2 * n + 1, 1)], min_val=0, max_val=WINS - 1)
                dve.wait_ge(s_gath[b], 16 * TILES * k)
                dve.wait_ge(s_we, n + 1)
                xs = xg[b][:, :, :].rearrange("p t (a c) -> p t a c", a=1).to_broadcast([P, TILES, C, C])
                nc.vector.tensor_tensor(prod[b % 2][:, :, :, :], we[b % 2][:, :, :].rearrange("p t (o i) -> p t o i", i=C),
                                        xs, ALU.mult).then_inc(s_prod, 1)
                dve.wait_ge(s_prod, n + 1)
                nc.vector.tensor_reduce(msg[b % 2][:, :, 0:C], prod[b % 2][:, :, :, :], axis=AX.X, op=ALU.add).then_inc(s_msg, 1)
                with dve.Fori(lo, hi + 1) as w:
                    dve.wait_ge(s_scat, dve.snap(made, min_val=0, max_val=NG * WINS))
                    for t in range(TILES):
                        oh = nc.vector.tensor_scalar(onehot[:, t, :], node_f[:, bass.ds(w * P, P)],
                                                     ix[b][:, TILES + t:TILES + t + 1], None, ALU.is_equal)
                    oh.then_inc(s_oh, 1)
                    dve.reg_add(made, made, 1)

            loop_groups(dve, step)
            dve.wait_ge(s_scat, dve.snap(made, min_val=0, max_val=NG * WINS))
            sums = acc[:, 0:WINS * MC].rearrange("p (w c) -> p w c", c=MC)
            link(nc.vector.tensor_scalar(stat[:, 0, :], sums[:, :, C], 1.0, None, ALU.max))
            link(nc.vector.reciprocal(stat[:, 3, :], stat[:, 0, :]))
            link(nc.vector.tensor_tensor(cen[:, :, :], sums[:, :, 0:C], wide(stat[:, 3, :]), ALU.mult))
            link(nc.vector.tensor_tensor(root_part[:, :, :], cen[:, :, :], root_part[:, :, :], ALU.add))
            norm(cen[:, :, :], root_part[:, :, :], 2)
            link(nc.vector.tensor_tensor(cen[:, :, :], cen[:, :, :], param(1), ALU.mult))
            link(nc.vector.tensor_tensor(cen[:, :, :], cen[:, :, :], param(2), ALU.add))
            nc.vector.tensor_tensor(cen[:, :, :], cen[:, :, :], xh[:, :, :], ALU.add).then_inc(s_pre, 1)
            dve.wait_ge(s_act, 1)
            nc.vector.tensor_tensor(cen[:, :, :], sq[:, :, :], x_in[:, :, :], ALU.add).then_inc(s_fin, 1)


def kernel(x, src, dst, edge_attr_8, L0_gnn_W1, L0_gnn_b1, L0_gnn_W2, L0_gnn_b2, L0_gnn_root, L0_gnn_bias,
           L0_gnn_ln_w, L0_gnn_ln_b):
    import numpy as np
    import concourse.bacc as bacc
    from concourse.bass_utils import run_bass_kernel_spmd as run

    pad = NG * GE - N_EDGES
    src_p = np.pad(np.asarray(src), (0, pad)).reshape(NG, TILES, P)
    dst_p = np.pad(np.asarray(dst), (0, pad), constant_values=PAD_DST).reshape(NG, TILES, P)
    ea_p = np.pad(np.asarray(edge_attr_8), ((0, pad), (0, 0))).reshape(NG, GE, ED)
    w2e = np.concatenate([np.asarray(L0_gnn_W2), np.asarray(L0_gnn_b2)[None, :]], 0).reshape(HID + 1, C, C)
    arrays = {
        "x": np.pad(np.asarray(x), ((0, WINS * P - N_NODES), (0, 0))),
        "edge_t": ea_p.transpose(0, 2, 1),
        "edge_ix": np.concatenate([src_p, dst_p], 1).transpose(0, 2, 1),
        "dst_rows": dst_p.reshape(NG, GE),
        "w1": np.asarray(L0_gnn_W1),
        "b1": np.asarray(L0_gnn_b1)[:, None],
        "w2e": w2e.transpose(0, 2, 1).reshape(HID + 1, C * C),
        "root": np.asarray(L0_gnn_root),
        "rows": np.broadcast_to(np.stack([np.asarray(L0_gnn_bias), np.asarray(L0_gnn_ln_w), np.asarray(L0_gnn_ln_b)]),
                                (P, 3, C)),
    }
    arrays = {k: np.ascontiguousarray(v) for k, v in arrays.items()}
    nc = bacc.Bacc("TRN2", target_bir_lowering=False, num_devices=1)
    aps = [nc.dram_tensor(k, v.shape, mybir.dt.from_np(v.dtype), kind="ExternalInput").ap() for k, v in arrays.items()]
    x_table = nc.dram_tensor("x_table", (WINS * P, C), mybir.dt.float32, kind="Internal").ap()
    span_table = nc.dram_tensor("span_table", (NG * 2,), mybir.dt.int32, kind="Internal").ap()
    out = nc.dram_tensor("out", (N_NODES, C), mybir.dt.float32, kind="ExternalOutput").ap()
    gnn_layer(nc, *aps, x_table, span_table, out)
    return run(nc, [arrays], core_ids=[0]).results[0]["out"]
```

```python
import concourse.bass as bass
from concourse import mybir
from contextlib import ExitStack

P = 128
N_NODES = 3125
N_EDGES = 100000
C = 16
ED = 8
HID = 64
TILES = 4
GE = TILES * P
NG = -(-N_EDGES // GE)
WINS = -(-N_NODES // P)
MC = C + 1
PAD_DST = WINS * P
BUFS = 4
EPS = 1e-5


def gnn_layer(nc, x, edge_t, edge_src, edge_dst, dst_rows, w1, b1, w2e, root, rows, x_table, span_table, out):
    fp32, i32 = mybir.dt.float32, mybir.dt.int32
    ALU, ACT, AX = mybir.AluOpType, mybir.ActivationFunctionType, mybir.AxisListType
    ROWS2 = NG // 2
    FULL = N_NODES // P
    REST = N_NODES - FULL * P
    KC = P // C
    CH = -(-WINS // KC)

    with ExitStack() as ctx:
        def sb(name, shape, dt=fp32):
            return ctx.enter_context(nc.sbuf_tensor(name, shape, dt))

        def ps(name, shape):
            return ctx.enter_context(nc.psum_tensor(name, shape, fp32))

        def sem(name):
            return ctx.enter_context(nc.semaphore(name))

        x_in = sb("x_in", [P, WINS, C])
        xh = sb("xh", [P, WINS, C])
        sq = sb("sq", [P, WINS, C])
        cen = sb("cen", [P, WINS, C])
        root_part = sb("root_part", [P, WINS, C])
        stat = sb("stat", [P, 4, WINS])
        row_params = sb("row_params", [P, 3, C])
        ident = sb("ident", [P, P])
        root_diag = sb("root_diag", [P, P])
        xT = sb("xT", [P, CH, P])
        node_i = sb("node_i", [P, WINS * P], i32)
        node_f = sb("node_f", [P, WINS * P])
        dst_sb = sb("dst_sb", [ROWS2, 2, GE], i32)
        span_f = sb("span_f", [ROWS2, 2, 2], i32)
        span_w = sb("span_w", [ROWS2, 2, 2], i32)
        spans = sb("spans", [1, NG * 2], i32)
        w1_sb = sb("w1_sb", [ED, HID])
        b1_sb = sb("b1_sb", [HID, 1])
        w2_sb = sb("w2_sb", [P, C * C])
        ea = [sb(f"ea{i}", [ED, GE]) for i in range(BUFS)]
        src_ix = [sb(f"src_ix{i}", [P, TILES], i32) for i in range(BUFS)]
        dst_ix = [sb(f"dst_ix{i}", [P, TILES], i32) for i in range(BUFS)]
        xg = [sb(f"xg{i}", [P, TILES, C]) for i in range(BUFS)]
        hT = [sb(f"hT{i}", [P, GE]) for i in range(2)]
        prod = [sb(f"prod{i}", [P, TILES, C, C]) for i in range(2)]
        msg = [sb(f"msg{i}", [P, TILES, MC]) for i in range(2)]
        onehot = [sb(f"onehot{i}", [P, TILES, P]) for i in range(2)]
        onehot_x = sb("onehot_x", [P, TILES, P])

        acc = ps("acc", [P, 512])
        hps = [ps(f"hps{i}", [P, 512]) for i in range(2)]
        we = [ps(f"we{i}", [P, TILES, C * C]) for i in range(2)]
        pT = ps("pT", [P, 512])

        s_x = sem("s_x")
        s_par = sem("s_par")
        s_w = sem("s_w")
        s_dst = sem("s_dst")
        s_ones = sem("s_ones")
        s_iota = sem("s_iota")
        s_id0 = sem("s_id0")
        s_id = sem("s_id")
        s_dz = sem("s_dz")
        s_diag = sem("s_diag")
        s_v = sem("s_v")
        s_var = sem("s_var")
        s_sd = sem("s_sd")
        s_xh = sem("s_xh")
        s_table = sem("s_table")
        s_xT = sem("s_xT")
        s_xTc = sem("s_xTc")
        s_root = sem("s_root")
        s_spanw = sem("s_spanw")
        s_spand = sem("s_spand")
        s_span = sem("s_span")
        s_ea = [sem(f"s_ea{i}") for i in range(BUFS)]
        s_src = [sem(f"s_src{i}") for i in range(BUFS)]
        s_dst_ix = [sem(f"s_dst_ix{i}") for i in range(BUFS)]
        s_gath = [sem(f"s_gath{i}") for i in range(BUFS)]
        s_hps = sem("s_hps")
        s_h = sem("s_h")
        s_we = sem("s_we")
        s_prod = sem("s_prod")
        s_msg = sem("s_msg")
        s_oh = sem("s_oh")
        s_first = sem("s_first")
        s_ohx = sem("s_ohx")
        s_scatx = sem("s_scatx")
        s_pre = sem("s_pre")
        s_act = sem("s_act")
        s_fin = sem("s_fin")
        s_out = sem("s_out")

        block = ctx.enter_context(nc.Block())

        def buf(n):
            return n % BUFS

        def rounds(n, b):
            return (n - b) // BUFS + 1

        def loop_groups(eng, step):
            for b in range(BUFS):
                step(b, b, b, False, 1)
            with eng.Fori(1, NG // BUFS - 1) as it:
                for b in range(BUFS):
                    step(it * BUFS + b, b, None, False, it + 1)
            for b in range(BUFS):
                step(NG - BUFS + b, b, None, b == BUFS - 1, NG // BUFS)

        @block.sync
        def _(sp):
            sp.dma_start(x_in[:, :, :], x.rearrange("(w p) c -> p w c", p=P)).then_inc(s_x, 16)
            sp.dma_start(row_params[:, :, :], rows).then_inc(s_par, 16)
            sp.dma_start(dst_sb[:, :, :], dst_rows.rearrange("(r h) e -> r h e", h=2)).then_inc(s_dst, 16)

            def load(n, b, early, last, k):
                if early is None:
                    sp.wait_ge(s_hps, n - BUFS + 1)
                sp.dma_start(ea[b][:, :], edge_t[bass.ds(n, 1), :, :].rearrange("a f e -> (a f) e")).then_inc(s_ea[b], 16)
                if early is None:
                    sp.wait_ge(s_gath[b], 16 * TILES * (k - 1))
                sp.dma_start(src_ix[b][:, :], edge_src[bass.ds(n, 1), :, :].rearrange("a p t -> (a p) t")).then_inc(s_src[b], 16)
                if early is None:
                    sp.wait_ge(s_prod, n - BUFS + 2)
                sp.dma_start(dst_ix[b][:, :], edge_dst[bass.ds(n, 1), :, :].rearrange("a p t -> (a p) t")).then_inc(s_dst_ix[b], 16)

            for b in range(BUFS):
                load(b, b, b, False, 1)
            sp.wait_ge(s_xh, 1)
            sp.dma_start(x_table.rearrange("(w p) c -> p w c", p=P), xh[:, :, :]).then_inc(s_table, 16)
            sp.wait_ge(s_spanw, 1)
            sp.dma_start(span_table.rearrange("(r k) -> r k", k=4), span_w[:, :, :].rearrange("r a b -> r (a b)")).then_inc(s_spand, 16)
            sp.wait_ge(s_spand, 16)
            sp.dma_start(spans[:, :], span_table.rearrange("(a k) -> a k", a=1)).then_inc(s_span, 16)
            with sp.Fori(1, NG // BUFS - 1) as it:
                for b in range(BUFS):
                    load(it * BUFS + b, b, None, False, it + 1)
            for b in range(BUFS):
                load(NG - BUFS + b, b, None, False, NG // BUFS)
            sp.wait_ge(s_table, 16)
            sp.wait_ge(s_fin, 1)
            sp.dma_start(out[0:FULL * P, :].rearrange("(w p) c -> p w c", p=P), cen[:, 0:FULL, :]).then_inc(s_out, 16)
            sp.dma_start(out[FULL * P:N_NODES, :], cen[0:REST, FULL, :]).then_inc(s_out, 16)
            sp.wait_ge(s_out, 32)

        @block.gpsimd
        def _(pool):
            nc.gpsimd.memset(ident[:, :], 0.0).then_inc(s_id0, 1)
            nc.gpsimd.memset(root_diag[:, :], 0.0).then_inc(s_dz, 1)
            pool.wait_ge(s_id0, 1)
            nc.gpsimd.affine_select(out=ident[:, :], in_=ident[:, :], compare_op=ALU.not_equal, fill=1.0,
                                    base=0, pattern=[[-1, P]], channel_multiplier=1).then_inc(s_id, 1)
            nc.gpsimd.iota(node_i[:, :], pattern=[[1, WINS * P]], base=0, channel_multiplier=0).then_inc(s_iota, 1)
            pool.wait_ge(s_table, 16)

            multiplied = pool.alloc_register("groups_multiplied")
            pool.reg_mov(multiplied, 1)

            def gather(n, b, early, last, k):
                if early is None and not isinstance(n, int):
                    so_far = pool.snap(multiplied, min_val=1, max_val=NG)
                    filled = pool.snap(16 * k)
                    pool.wait_ge(s_src[b], filled)
                    pool.wait_ge(s_prod, so_far)
                    pool.reg_add(multiplied, multiplied, 1)
                else:
                    pool.wait_ge(s_src[b], 16 * k)
                    if early is None:
                        pool.wait_ge(s_prod, n - BUFS + 1)
                for t in range(TILES):
                    pool.indirect_dma_start(
                        out=xg[b][:, t, :], out_offset=None, in_=x_table,
                        in_offset=bass.IndirectOffsetOnAxis(ap=src_ix[b][:, t:t + 1], axis=0)).then_inc(s_gath[b], 16)

            loop_groups(pool, gather)

        @block.scalar
        def _(act):
            act.dma_start(w1_sb[:, :], w1).then_inc(s_w, 16)
            act.dma_start(b1_sb[:, :], b1).then_inc(s_w, 16)
            act.wait_ge(s_ones, 1)
            act.dma_start(w2_sb[0:HID + 1, :], w2e).then_inc(s_w, 16)
            act.wait_ge(s_dz, 1)
            for k in range(KC):
                act.dma_start(root_diag[k * C:(k + 1) * C, k * C:(k + 1) * C], root).then_inc(s_diag, 16)
            act.wait_ge(s_var, 1)
            nc.scalar.activation(stat[:, 2, :], stat[:, 1, :], ACT.Sqrt).then_inc(s_sd, 1)
            act.wait_ge(s_w, 48)

            def silu(n, b, early, last, k):
                act.wait_ge(s_hps, n + 1)
                if early is None or early >= 2:
                    act.wait_ge(s_we, n - 1)
                nc.scalar.activation(hT[b % 2][0:HID, :], hps[b % 2][0:HID, :], ACT.Silu,
                                     bias=b1_sb[:, 0:1]).then_inc(s_h, 1)

            loop_groups(act, silu)
            act.wait_ge(s_var, 2)
            nc.scalar.activation(stat[:, 2, :], stat[:, 1, :], ACT.Sqrt).then_inc(s_sd, 1)
            act.wait_ge(s_pre, 1)
            nc.scalar.activation(sq[:, :, :], cen[:, :, :], ACT.Silu).then_inc(s_act, 1)

        @block.tensor
        def _(pe):
            pe.wait_ge(s_xh, 1)
            pe.wait_ge(s_id, 1)
            xh_flat = xh[:, :, :].rearrange("p w c -> p (w c)")
            for k in range(CH):
                cols = min(P, WINS * C - k * P)
                last = nc.tensor.transpose(pT[0:cols, k * P:(k + 1) * P], xh_flat[:, k * P:k * P + cols], ident[:, :])
            last.then_inc(s_xT, 1)
            pe.wait_ge(s_xTc, 1)
            pe.wait_ge(s_diag, 16 * KC)
            for k in range(CH):
                cols = min(P, WINS * C - k * P)
                last = nc.tensor.matmul(pT[:, k * P:k * P + cols], xT[0:cols, k, :], root_diag[0:cols, 0:cols],
                                        start=True, stop=True)
            last.then_inc(s_root, 1)

            def hidden(n, b, early, k):
                pe.wait_ge(s_ea[b], 16 * k)
                if early is None or early >= 2:
                    pe.wait_ge(s_h, n - 1)
                nc.tensor.matmul(hps[b % 2][0:HID, :], w1_sb[:, :], ea[b][:, :], start=True, stop=True).then_inc(s_hps, 1)

            def edge_matrices(n, b, early):
                pe.wait_ge(s_h, n + 1)
                if early is None or early >= 2:
                    pe.wait_ge(s_prod, n - 1)
                for t in range(TILES):
                    last = nc.tensor.matmul(we[b % 2][:, t, :], hT[b % 2][:, t * P:(t + 1) * P], w2_sb[:, :],
                                            start=True, stop=True)
                last.then_inc(s_we, 1)

            def add_window(hot, b, w):
                for t in range(TILES):
                    last = nc.tensor.matmul(acc[:, bass.ds(w * MC, MC)], hot[:, t, :], msg[b % 2][:, t, :],
                                            start=False, stop=False, skip_group_check=True)
                return last

            def scatter(n, b):
                lo = pe.value_load(spans[0:1, bass.ds(2 * n, 1)], min_val=0, max_val=WINS - 1)
                hi = pe.value_load(spans[0:1, bass.ds(2 * n + 1, 1)], min_val=0, max_val=WINS - 1)
                if isinstance(n, int):
                    pe.wait_ge(s_msg, n + 1)
                else:
                    pe.wait_ge(s_msg, pe.snap(messages, min_val=BUFS, max_val=NG))
                    pe.reg_add(messages, messages, 1)
                pe.wait_ge(s_oh, n + 1)
                add_window(onehot[b % 2], b, lo).then_inc(s_first, 1)
                with pe.If(hi - lo):
                    with pe.Fori(lo + 1, hi + 1) as w:
                        pe.reg_add(done, done, 1)
                        pe.wait_ge(s_ohx, pe.snap(done, min_val=1, max_val=NG * WINS))
                        add_window(onehot_x, b, w).then_inc(s_scatx, 1)

            pe.wait_ge(s_w, 48)
            pe.wait_ge(s_ones, 6)
            pe.wait_ge(s_span, 16)
            done = pe.alloc_register("windows_done")
            pe.reg_mov(done, 0)
            messages = pe.alloc_register("message_groups")
            pe.reg_mov(messages, BUFS)
            hidden(0, 0, 0, 1)

            def step(n, b, early, last, k):
                if not last:
                    nb = (b + 1) % BUFS
                    hidden(n + 1, nb, None if early is None or early == BUFS - 1 else early + 1,
                           k + 1 if nb == 0 else k)
                edge_matrices(n, b, early)
                if early != 0:
                    scatter(n - 1, (b - 1) % BUFS)

            loop_groups(pe, step)
            scatter(NG - 1, BUFS - 1)

        @block.vector
        def _(dve):
            chain = [0]

            def link(ins):
                chain[0] += 1
                ins.then_inc(s_v, 1)
                dve.wait_ge(s_v, chain[0])

            def wide(ap, k=C):
                return ap.rearrange("p (w a) -> p w a", a=1).to_broadcast([P, WINS, k])

            def norm(dst, src, sd_at):
                link(nc.vector.tensor_reduce(stat[:, 0, :], src, axis=AX.X, op=ALU.add))
                link(nc.vector.tensor_scalar(stat[:, 3, :], stat[:, 0, :], 1.0 / C, None, ALU.mult))
                link(nc.vector.tensor_tensor(dst, src, wide(stat[:, 3, :]), ALU.subtract))
                link(nc.vector.tensor_tensor(sq[:, :, :], dst, dst, ALU.mult))
                link(nc.vector.tensor_reduce(stat[:, 0, :], sq[:, :, :], axis=AX.X, op=ALU.add))
                nc.vector.tensor_scalar(stat[:, 1, :], stat[:, 0, :], 1.0 / C, EPS, ALU.mult, ALU.add).then_inc(s_var, 1)
                dve.wait_ge(s_sd, sd_at)
                link(nc.vector.reciprocal(stat[:, 3, :], stat[:, 2, :]))
                link(nc.vector.tensor_tensor(dst, dst, wide(stat[:, 3, :]), ALU.mult))

            nc.vector.memset(w2_sb[HID:P, :], 0.0).then_inc(s_ones, 1)
            for i in range(2):
                link(nc.vector.memset(hT[i][HID:P, :], 0.0))
                nc.vector.memset(hT[i][HID:HID + 1, :], 1.0).then_inc(s_ones, 1)
            dve.wait_ge(s_x, 16)
            norm(cen[:, :, :], x_in[:, :, :], 1)
            nc.vector.tensor_scalar(xh[:, :, :], cen[:, :, :], 0.0, None, ALU.max).then_inc(s_xh, 1)
            dve.wait_ge(s_dst, 16)
            nc.vector.tensor_reduce(span_f[:, :, 0], dst_sb[:, :, :], axis=AX.X, op=ALU.min)
            link(nc.vector.tensor_reduce(span_f[:, :, 1], dst_sb[:, :, :], axis=AX.X, op=ALU.max))
            link(nc.vector.tensor_scalar(span_f[:, :, :], span_f[:, :, :], float(N_NODES - 1), None, ALU.min))
            nc.vector.tensor_scalar(span_w[:, :, :], span_f[:, :, :], 7, None, ALU.arith_shift_right).then_inc(s_spanw, 1)
            nc.vector.memset(acc[:, :], 0.0).then_inc(s_ones, 1)
            for i in range(2):
                nc.vector.memset(msg[i][:, :, C:MC], 1.0).then_inc(s_ones, 1)
            dve.wait_ge(s_iota, 1)
            link(nc.vector.tensor_copy(node_f[:, :], node_i[:, :]))
            dve.wait_ge(s_xT, 1)
            full = (WINS * C) // P
            nc.vector.tensor_copy(xT[:, 0:full, :], pT[:, 0:full * P].rearrange("p (k n) -> p k n", n=P))
            rest = WINS * C - full * P
            nc.vector.tensor_copy(xT[0:rest, full, :], pT[0:rest, full * P:(full + 1) * P]).then_inc(s_xTc, 1)
            dve.wait_ge(s_root, 1)
            dve.wait_ge(s_par, 16)

            def param(k):
                return row_params[:, k:k + 1, :].to_broadcast([P, WINS, C])

            link(nc.vector.tensor_tensor(root_part[:, :, :], pT[:, 0:WINS * C].rearrange("p (w c) -> p w c", c=C),
                                         param(0), ALU.add))
            dve.wait_ge(s_span, 16)
            made = dve.alloc_register("windows_made")
            dve.reg_mov(made, 0)

            def one_hots(hot, b, w):
                for t in range(TILES):
                    last = nc.vector.tensor_scalar(hot[:, t, :], node_f[:, bass.ds(w * P, P)],
                                                   dst_ix[b][:, t:t + 1], None, ALU.is_equal)
                return last

            def step(n, b, early, last, k):
                lo = dve.value_load(spans[0:1, bass.ds(2 * n, 1)], min_val=0, max_val=WINS - 1)
                hi = dve.value_load(spans[0:1, bass.ds(2 * n + 1, 1)], min_val=0, max_val=WINS - 1)
                dve.wait_ge(s_gath[b], 16 * TILES * k)
                dve.wait_ge(s_we, n + 1)
                xs = xg[b][:, :, :].rearrange("p t (a c) -> p t a c", a=1).to_broadcast([P, TILES, C, C])
                nc.vector.tensor_tensor(prod[b % 2][:, :, :, :], we[b % 2][:, :, :].rearrange("p t (o i) -> p t o i", i=C),
                                        xs, ALU.mult).then_inc(s_prod, 1)
                dve.wait_ge(s_dst_ix[b], 16 * k)
                if early is None or early >= 2:
                    dve.wait_ge(s_first, n - 1)
                one_hots(onehot[b % 2], b, lo).then_inc(s_oh, 1)
                dve.wait_ge(s_prod, n + 1)
                nc.vector.tensor_reduce(msg[b % 2][:, :, 0:C], prod[b % 2][:, :, :, :], axis=AX.X, op=ALU.add).then_inc(s_msg, 1)
                with dve.If(hi - lo):
                    with dve.Fori(lo + 1, hi + 1) as w:
                        dve.wait_ge(s_scatx, dve.snap(made, min_val=0, max_val=NG * WINS))
                        one_hots(onehot_x, b, w).then_inc(s_ohx, 1)
                        dve.reg_add(made, made, 1)

            loop_groups(dve, step)
            dve.wait_ge(s_first, NG)
            dve.wait_ge(s_scatx, dve.snap(made, min_val=0, max_val=NG * WINS))
            sums = acc[:, 0:WINS * MC].rearrange("p (w c) -> p w c", c=MC)
            link(nc.vector.tensor_scalar(stat[:, 0, :], sums[:, :, C], 1.0, None, ALU.max))
            link(nc.vector.reciprocal(stat[:, 3, :], stat[:, 0, :]))
            link(nc.vector.tensor_tensor(cen[:, :, :], sums[:, :, 0:C], wide(stat[:, 3, :]), ALU.mult))
            link(nc.vector.tensor_tensor(root_part[:, :, :], cen[:, :, :], root_part[:, :, :], ALU.add))
            norm(cen[:, :, :], root_part[:, :, :], 2)
            link(nc.vector.tensor_tensor(cen[:, :, :], cen[:, :, :], param(1), ALU.mult))
            link(nc.vector.tensor_tensor(cen[:, :, :], cen[:, :, :], param(2), ALU.add))
            nc.vector.tensor_tensor(cen[:, :, :], cen[:, :, :], xh[:, :, :], ALU.add).then_inc(s_pre, 1)
            dve.wait_ge(s_act, 1)
            nc.vector.tensor_tensor(cen[:, :, :], sq[:, :, :], x_in[:, :, :], ALU.add).then_inc(s_fin, 1)


def kernel(x, src, dst, edge_attr_8, L0_gnn_W1, L0_gnn_b1, L0_gnn_W2, L0_gnn_b2, L0_gnn_root, L0_gnn_bias,
           L0_gnn_ln_w, L0_gnn_ln_b):
    import numpy as np
    import concourse.bacc as bacc
    from concourse.bass_utils import run_bass_kernel_spmd as run

    pad = NG * GE - N_EDGES
    src_p = np.pad(np.asarray(src), (0, pad)).reshape(NG, TILES, P)
    dst_p = np.pad(np.asarray(dst), (0, pad), constant_values=PAD_DST).reshape(NG, TILES, P)
    ea_p = np.pad(np.asarray(edge_attr_8), ((0, pad), (0, 0))).reshape(NG, GE, ED)
    w2e = np.concatenate([np.asarray(L0_gnn_W2), np.asarray(L0_gnn_b2)[None, :]], 0).reshape(HID + 1, C, C)
    arrays = {
        "x": np.pad(np.asarray(x), ((0, WINS * P - N_NODES), (0, 0))),
        "edge_t": ea_p.transpose(0, 2, 1),
        "edge_src": src_p.transpose(0, 2, 1),
        "edge_dst": dst_p.transpose(0, 2, 1),
        "dst_rows": dst_p.reshape(NG, GE),
        "w1": np.asarray(L0_gnn_W1),
        "b1": np.asarray(L0_gnn_b1)[:, None],
        "w2e": w2e.transpose(0, 2, 1).reshape(HID + 1, C * C),
        "root": np.asarray(L0_gnn_root),
        "rows": np.broadcast_to(np.stack([np.asarray(L0_gnn_bias), np.asarray(L0_gnn_ln_w), np.asarray(L0_gnn_ln_b)]),
                                (P, 3, C)),
    }
    arrays = {k: np.ascontiguousarray(v) for k, v in arrays.items()}
    nc = bacc.Bacc("TRN2", target_bir_lowering=False, num_devices=1)
    aps = [nc.dram_tensor(k, v.shape, mybir.dt.from_np(v.dtype), kind="ExternalInput").ap() for k, v in arrays.items()]
    x_table = nc.dram_tensor("x_table", (WINS * P, C), mybir.dt.float32, kind="Internal").ap()
    span_table = nc.dram_tensor("span_table", (NG * 2,), mybir.dt.int32, kind="Internal").ap()
    out = nc.dram_tensor("out", (N_NODES, C), mybir.dt.float32, kind="ExternalOutput").ap()
    gnn_layer(nc, *aps, x_table, span_table, out)
    return run(nc, [arrays], core_ids=[0]).results[0]["out"]
```

```python
import concourse.bass as bass
from concourse import mybir
from contextlib import ExitStack

P = 128
N_NODES = 3125
N_EDGES = 100000
C = 16
ED = 8
HID = 64
HALVES = P // HID
TILES = 4
GE = TILES * P
HE = GE // HALVES
NG = -(-N_EDGES // GE)
WINS = -(-N_NODES // P)
SUMS = WINS * P
PAD_DST = SUMS
PICKS = (1, 1, 1, 1, 1, 1, 1, 2)
PAIR = 2
BUFS = 8
PAIRS = BUFS // PAIR
CYCLE = len(PICKS) // PAIR
AHEAD = 3
SPAN = 40
MC = 2 * C + 1
BANK = 512
LOW = 256
CHUNKS = LOW // P
HIGHS = -(-N_NODES // LOW)
SCALE = 2.0 ** 13
FLOOR = -8.0
EPS = 1e-5


def gnn_layer(nc, x, edge_t, edge_nodes, pick_src, dst_rows, w1_rows, w2_rows, root_rows, close_rows, rows,
              x_table, span_table, out):
    fp32, i32, fp16, u8 = mybir.dt.float32, mybir.dt.int32, mybir.dt.float16, mybir.dt.uint8
    ALU, ACT, AX = mybir.AluOpType, mybir.ActivationFunctionType, mybir.AxisListType
    PAIRS_ALL = NG // PAIR
    FULL = N_NODES // P
    REST = N_NODES - FULL * P
    KC = P // C
    CH = -(-WINS // KC)
    EROWS = HALVES * ED + 1
    AC = C + 1
    PARTS = (slice(0, 16), slice(16, WINS))

    with ExitStack() as ctx:
        def sb(name, shape, dt=fp32):
            return ctx.enter_context(nc.sbuf_tensor(name, shape, dt))

        def ps(name, shape):
            return ctx.enter_context(nc.psum_tensor(name, shape, fp32))

        def sem(name):
            return ctx.enter_context(nc.semaphore(name))

        def fetched(b):
            return TILES - PICKS[b % len(PICKS)]

        def picks_before(b):
            return sum(PICKS[i % len(PICKS)] for i in range(b - b % PAIR, b))

        def pair_picks(q):
            return sum(PICKS[i % len(PICKS)] for i in range(q * PAIR, (q + 1) * PAIR))

        x_in = sb("x_in", [P, WINS, C])
        xh = sb("xh", [P, WINS, C])
        xh_b = sb("xh_b", [P, WINS, C])
        sq = sb("sq", [P, WINS, C])
        cen = sb("cen", [P, WINS, C])
        root_part = sb("root_part", [P, WINS, C])
        stat = sb("stat", [P, 3, WINS])
        one = sb("one", [P, 1])
        eps = sb("eps", [P, 1])
        warm = sb("warm", [P, 1])
        row_params = sb("row_params", [P, 3, C])
        ident = sb("ident", [P, P])
        root_diag = sb("root_diag", [P, P])
        close = sb("close", [MC, AC])
        xT = sb("xT", [P, CH, P])
        node_i = sb("node_i", [P, SUMS], i32)
        dst_sb = sb("dst_sb", [PAIRS_ALL, 2, GE], i32)
        span_f = sb("span_f", [PAIRS_ALL, 2, 2], i32)
        span_w = sb("span_w", [PAIRS_ALL, 2, PAIR], i32)
        spans = sb("spans", [1, NG * 2], i32)
        w1_diag = sb("w1_diag", [P, P])
        w2_diag = sb("w2_diag", [P, HALVES * C * C])
        xh_scaled = sb("xh_scaled", [P, WINS, C])
        pick_hi = sb("pick_hi", [P, CHUNKS, C, HIGHS], fp16)
        pick_lo = sb("pick_lo", [P, CHUNKS, C, HIGHS], fp16)
        lower_f = sb("lower_f", [HIGHS, C, HIGHS])
        lower = sb("lower", [HIGHS, C, HIGHS], fp16)
        minus_i = sb("minus_i", [P, CHUNKS], i32)
        minus = sb("minus", [P, CHUNKS])
        tiny = sb("tiny", [P, 1])

        ea = [sb(f"ea{i}", [P, PAIR, HE]) for i in range(PAIRS)]
        nodes = [sb(f"nodes{i}", [P, 2, PAIR, TILES], i32) for i in range(PAIRS)]
        mx = [sb(f"mx{i}", [P, TILES, MC]) for i in range(BUFS)]
        pick_ix = [sb(f"pick_ix{i}", [P, pair_picks(i) * P], i32) for i in range(PAIRS)]
        most = max(pair_picks(q) for q in range(PAIRS)) * P
        low_away = sb("low_away", [P, CHUNKS, most], fp16)
        high_away = sb("high_away", [HIGHS, most], fp16)
        low_hot = [sb(f"low_hot{i}", [P, CHUNKS, pair_picks(i) * P], fp16) for i in range(PAIRS)]
        high_hot = [sb(f"high_hot{i}", [HIGHS, pair_picks(i) * P], fp16) for i in range(PAIRS)]
        hT = [sb(f"hT{i}", [P, HE]) for i in range(2)]
        prod = [sb(f"prod{i}", [P, TILES, C, C]) for i in range(2)]
        onehot = [sb(f"onehot{i}", [P, TILES, SPAN]) for i in range(BUFS)]
        onehot_x = sb("onehot_x", [P, TILES, SPAN])
        acc = sb("acc", [MC, SUMS])

        sums = [ps(f"sums{i}", [P, BANK]) for i in range(2)]
        hps = ps("hps", [P, BANK])
        picked = ps("picked", [P, BANK])
        we = [ps(f"we{i}", [P, TILES, C * C]) for i in range(2)]
        pT = we[1][:, 0:2, :].rearrange("p t c -> p (t c)")
        closed = [we[0][:, 2 * i:2 * i + 2, :].rearrange("p t c -> p (t c)")[:, 0:(part.stop - part.start) * AC]
                  .rearrange("p (w c) -> p w c", c=AC) for i, part in enumerate(PARTS)]

        s_x = sem("s_x")
        s_par = sem("s_par")
        s_w = sem("s_w")
        s_dst = sem("s_dst")
        s_one = sem("s_one")
        s_ones = sem("s_ones")
        s_warm = sem("s_warm")
        s_eaz = sem("s_eaz")
        s_iota = sem("s_iota")
        s_id0 = sem("s_id0")
        s_id = sem("s_id")
        s_low = sem("s_low")
        s_byte = sem("s_byte")
        s_minus = sem("s_minus")
        s_diag = sem("s_diag")
        s_close = sem("s_close")
        s_v = sem("s_v")
        s_var = sem("s_var")
        s_sd = sem("s_sd")
        s_xh = sem("s_xh")
        s_table = sem("s_table")
        s_tables = sem("s_tables")
        s_xT = sem("s_xT")
        s_xTc = sem("s_xTc")
        s_root = sem("s_root")
        s_rootc = sem("s_rootc")
        s_spanw = sem("s_spanw")
        s_spand = sem("s_spand")
        s_span = sem("s_span")
        s_ea = [sem(f"s_ea{i}") for i in range(PAIRS)]
        s_nodes = [sem(f"s_nodes{i}") for i in range(PAIRS)]
        s_gath = [sem(f"s_gath{i}") for i in range(BUFS)]
        s_pix = [sem(f"s_pix{i}") for i in range(PAIRS)]
        s_away = sem("s_away")
        s_hots = sem("s_hots")
        s_pick = sem("s_pick")
        s_sel = sem("s_sel")
        s_hps = sem("s_hps")
        s_h = sem("s_h")
        s_we = sem("s_we")
        s_prod = sem("s_prod")
        s_msg = sem("s_msg")
        s_oh = sem("s_oh")
        s_sum = sem("s_sum")
        s_ohx = sem("s_ohx")
        s_sumx = sem("s_sumx")
        s_acc = sem("s_acc")
        s_accx = sem("s_accx")
        s_settled = sem("s_settled")
        s_all = sem("s_all")
        s_closed = sem("s_closed")
        s_pre = sem("s_pre")
        s_act = sem("s_act")
        s_fin = sem("s_fin")
        s_out = sem("s_out")

        block = ctx.enter_context(nc.Block())

        ROUNDS = NG // BUFS
        FURTHER = 1

        def ahead(n, b, early, k, m):
            new = early + m if early is not None and early + m < BUFS else None
            return n + m, (b + m) % BUFS, new, k + (b + m) // BUFS

        def loop_groups(eng, step):
            for n in range(BUFS):
                step(n, n, n, 1)
            with eng.Fori(1, ROUNDS) as it:
                for b in range(BUFS):
                    step(it * BUFS + b, b, None, it + 1)
            for n in range(ROUNDS * BUFS, NG):
                step(n, n % BUFS, None, n // BUFS + 1)

        def groups_left(n):
            return NG - 1 - n if isinstance(n, int) else NG

        def as_node(eng, register):
            return eng.snap(register, min_val=0, max_val=N_NODES - 1)

        def as_count(eng, register):
            return eng.snap(register, min_val=0, max_val=N_NODES // SPAN)

        @block.sync
        def _(sp):
            sp.dma_start(x_in[:, :, :], x.rearrange("(w p) c -> p w c", p=P)).then_inc(s_x, 16)

            def load_nodes(q, early, k):
                m = (k - 1) * PAIRS + q
                if not early:
                    sp.wait_ge(s_prod, (m - PAIRS) * PAIR + 2 * PAIR)
                sp.dma_start(nodes[q][:, :, :, :], edge_nodes[bass.ds(m, 1), :, :, :, :]
                             .rearrange("a p s g t -> (a p) s g t")).then_inc(s_nodes[q], 16)

            def load_features(q, early, k):
                m = (k - 1) * PAIRS + q
                if not early:
                    sp.wait_ge(s_hots, m - PAIRS + 1)
                first = sum(pair_picks(i) for i in range(q - q % CYCLE, q)) * P
                count = pair_picks(q) * P
                sp.dma_start(pick_ix[q][:, :], pick_src[bass.ds((k - 1) * (PAIRS // CYCLE) + q // CYCLE, 1), first:first + count]
                             .to_broadcast([P, count])).then_inc(s_pix[q], 16)
                if not early:
                    sp.wait_ge(s_hps, (m - PAIRS) * PAIR + PAIR)
                sp.dma_start(ea[q][0:EROWS, :, :], edge_t[bass.ds(m, 1), :, :, :]
                             .rearrange("a f g e -> (a f) g e")).then_inc(s_ea[q], 16)

            load_nodes(0, True, 1)
            sp.wait_ge(s_eaz, PAIRS)
            load_features(0, True, 1)
            load_nodes(1, True, 1)
            sp.wait_ge(s_xh, 1)
            sp.dma_start(x_table.rearrange("(w p) c -> p w c", p=P), xh[:, :, :]).then_inc(s_table, 16)
            load_features(1, True, 1)
            sp.wait_ge(s_spanw, 1)
            sp.dma_start(span_table.rearrange("(r k) -> r k", k=4), span_w[:, :, :].rearrange("r a b -> r (a b)")).then_inc(s_spand, 16)
            sp.wait_ge(s_spand, 16)
            sp.dma_start(spans[:, :], span_table.rearrange("(a k) -> a k", a=1)).then_inc(s_span, 16)
            for q in range(2, PAIRS):
                load_nodes(q, True, 1)
                load_features(q, True, 1)
            with sp.Fori(1, ROUNDS) as it:
                for q in range(PAIRS):
                    load_features(q, False, it + 1)
                    load_nodes(q, False, it + 1)
            for m in range(ROUNDS * PAIRS, NG // PAIR):
                load_features(m % PAIRS, False, m // PAIRS + 1)
                load_nodes(m % PAIRS, False, m // PAIRS + 1)
            sp.wait_ge(s_table, 16)
            for i, part in enumerate(PARTS):
                sp.wait_ge(s_fin, 1 + i)
                full = min(part.stop, FULL)
                sp.dma_start(out[part.start * P:full * P, :].rearrange("(w p) c -> p w c", p=P),
                             cen[:, part.start:full, :]).then_inc(s_out, 16)
            sp.dma_start(out[FULL * P:N_NODES, :], cen[0:REST, FULL, :]).then_inc(s_out, 16)
            sp.wait_ge(s_out, 16 * (len(PARTS) + 1))

        @block.gpsimd
        def _(pool):
            for q in range(PAIRS):
                nc.gpsimd.memset(ea[q][:, :, :], 0.0).then_inc(s_eaz, 1)
            nc.gpsimd.memset(ident[:, :], 0.0).then_inc(s_id0, 1)
            nc.gpsimd.memset(lower_f[:, :, :], FLOOR).then_inc(s_id0, 1)
            nc.gpsimd.iota(minus_i[:, :], pattern=[[-P, CHUNKS]], base=0, channel_multiplier=-1).then_inc(s_byte, 1)
            pool.wait_ge(s_id0, 2)
            nc.gpsimd.affine_select(out=ident[:, :], in_=ident[:, :], compare_op=ALU.not_equal, fill=1.0,
                                    base=0, pattern=[[-1, P]], channel_multiplier=1).then_inc(s_id, 1)
            nc.gpsimd.affine_select(out=lower_f[:, :, :], in_=lower_f[:, :, :], compare_op=ALU.not_equal, fill=0.0,
                                    base=0, pattern=[[0, C], [-1, HIGHS]], channel_multiplier=1).then_inc(s_low, 1)
            nc.gpsimd.iota(node_i[:, :], pattern=[[1, SUMS]], base=0, channel_multiplier=0).then_inc(s_iota, 1)
            added = pool.alloc_register("groups_added")
            pool.reg_mov(added, 5)
            pool.wait_ge(s_table, 16)

            def gather(n, b, early, k):
                q, g = b // PAIR, b % PAIR
                if early is None and not isinstance(n, int):
                    so_far = pool.snap(pool.snap(added, min_val=1, max_val=NG) - g)
                    if g == 0:
                        filled = pool.snap(16 * k)
                        pool.wait_ge(s_nodes[q], filled)
                    pool.wait_ge(s_hps, so_far)
                    pool.reg_add(added, added, 1)
                else:
                    if g == 0:
                        pool.wait_ge(s_nodes[q], 16 * k)
                    if early is None:
                        pool.wait_ge(s_hps, n - BUFS + 5 - g)
                for t in range(fetched(b)):
                    pool.indirect_dma_start(
                        out=mx[b][:, t, C + 1:MC], out_offset=None, in_=x_table,
                        in_offset=bass.IndirectOffsetOnAxis(ap=nodes[q][:, 0, g, t:t + 1], axis=0)).then_inc(s_gath[b], 16)

            loop_groups(pool, gather)

        @block.scalar
        def _(act):
            act.dma_start(dst_sb[:, :, :], dst_rows.rearrange("(r h) e -> r h e", h=2)).then_inc(s_dst, 16)
            act.dma_start(w1_diag[:, :], w1_rows).then_inc(s_w, 16)
            act.dma_start(w2_diag[:, :], w2_rows).then_inc(s_w, 16)
            act.wait_ge(s_one, 3)
            nc.scalar.activation(warm[:, 0:1], one[:, :], ACT.Sqrt).then_inc(s_warm, 1)
            act.dma_start(root_diag[:, :], root_rows).then_inc(s_diag, 16)
            act.dma_start(row_params[:, :, :], rows).then_inc(s_par, 16)
            act.dma_start(close[:, :], close_rows).then_inc(s_close, 16)
            act.wait_ge(s_var, 1)
            nc.scalar.activation(stat[:, 1, :], stat[:, 0, :], ACT.Sqrt, scale=1.0 / C, bias=eps[:, :]).then_inc(s_sd, 1)
            act.wait_ge(s_warm, 1)
            nc.scalar.activation(warm[:, 0:1], one[:, :], ACT.Silu).then_inc(s_warm, 1)

            def pick_hots(n, b, early, k):
                q = b // PAIR
                act.wait_ge(s_pix[q], 16 * k)
                if early is None or early >= PAIR:
                    act.wait_ge(s_hots, (k - 1) * PAIRS + q)
                byte = pick_ix[q][:, :].bitcast(u8).rearrange("p (e k) -> p k e", k=4)
                count = pair_picks(q) * P
                for c in range(CHUNKS):
                    nc.scalar.activation(low_away[:, c, 0:count], byte[:, 0, :], ACT.Abs, bias=minus[:, c:c + 1])
                nc.scalar.activation(high_away[:, 0:count], byte[0:HIGHS, 1, :], ACT.Abs, bias=minus[0:HIGHS, 0:1]).then_inc(s_away, 1)
                if early is None:
                    act.wait_ge(s_pick, n - BUFS + PAIR)
                act.wait_ge(s_away, (k - 1) * PAIRS + (q + 1))
                nc.scalar.activation(low_hot[q][:, :, :], low_away[:, :, 0:count], ACT.Relu, bias=tiny[:, :], scale=-1.0 / SCALE)
                nc.scalar.activation(high_hot[q][:, :], high_away[:, 0:count], ACT.Relu, bias=one[0:HIGHS, :],
                                     scale=-1.0).then_inc(s_hots, 1)

            def hidden(n, b, early, k):
                act.wait_ge(s_hps, n + 1)
                if early is None or early >= 2:
                    act.wait_ge(s_we, n - 1)
                nc.scalar.activation(hT[b % 2][:, :], hps[:, 0:HE], ACT.Silu).then_inc(s_h, 1)

            def step(n, b, early, k):
                if groups_left(n) >= 1:
                    hidden(*ahead(n, b, early, k, 1))
                if (b + AHEAD) % PAIR == 0 and groups_left(n) >= AHEAD:
                    pick_hots(*ahead(n, b, early, k, AHEAD))

            hidden(0, 0, 0, 1)
            act.wait_ge(s_minus, 1)
            pick_hots(0, 0, 0, 1)
            pick_hots(PAIR, PAIR, PAIR, 1)
            loop_groups(act, step)
            act.wait_ge(s_warm, 2)
            nc.scalar.activation(warm[:, 0:1], one[:, :], ACT.Sqrt).then_inc(s_warm, 1)
            for i, part in enumerate(PARTS):
                act.wait_ge(s_var, 2 + i)
                nc.scalar.activation(stat[:, 1, part], stat[:, 0, part], ACT.Sqrt, scale=1.0 / C, bias=eps[:, :]).then_inc(s_sd, 1)
            act.wait_ge(s_warm, 3)
            nc.scalar.activation(warm[:, 0:1], one[:, :], ACT.Silu).then_inc(s_warm, 1)
            for i, part in enumerate(PARTS):
                act.wait_ge(s_pre, 1 + i)
                nc.scalar.activation(sq[:, part, :], cen[:, part, :], ACT.Silu).then_inc(s_act, 1)

        @block.tensor
        def _(pe):
            pe.wait_ge(s_xh, 1)
            pe.wait_ge(s_id, 1)
            flat = xh[:, :, :].rearrange("p w c -> p (w c)")
            for k in range(CH):
                cols = min(P, WINS * C - k * P)
                nc.tensor.transpose(pT[0:cols, k * P:(k + 1) * P], flat[:, k * P:k * P + cols],
                                    ident[:, :]).then_inc(s_xT, 1)

            def root_product():
                pe.wait_ge(s_xTc, 1)
                pe.wait_ge(s_diag, 16)
                for k in range(CH):
                    cols = min(P, WINS * C - k * P)
                    nc.tensor.matmul(pT[:, k * P:k * P + cols], xT[0:cols, k, :], root_diag[0:cols, 0:cols],
                                     start=True, stop=True).then_inc(s_root, 1)

            def hidden(n, b, early, k):
                if b % PAIR == 0:
                    pe.wait_ge(s_ea[b // PAIR], 16 * k)
                if early is None or early >= 1:
                    pe.wait_ge(s_h, n)
                nc.tensor.matmul(hps[:, 0:HE], w1_diag[:, :], ea[b // PAIR][:, b % PAIR, :], start=True, stop=True).then_inc(s_hps, 1)

            def edge_matrices(n, b, early, k):
                pe.wait_ge(s_h, n + 1)
                if early is None or early >= 2:
                    pe.wait_ge(s_prod, n - 1)
                for j in range(TILES // HALVES):
                    last = nc.tensor.matmul(we[b % 2][:, HALVES * j:HALVES * (j + 1), :], hT[b % 2][:, j * P:(j + 1) * P],
                                            w2_diag[:, :], start=True, stop=True)
                last.then_inc(s_we, 1)

            def pick(n, b, early, k):
                q = b // PAIR
                if b % PAIR == 0:
                    pe.wait_ge(s_hots, (k - 1) * PAIRS + (q + 1))
                if early is None or early >= 1:
                    pe.wait_ge(s_sel, n)
                for i in range(TILES - fetched(b)):
                    at = (picks_before(b) + i) * P
                    to = picked[:, i * C * HIGHS:(i + 1) * C * HIGHS]
                    for c in range(CHUNKS):
                        for part in (pick_hi, pick_lo):
                            nc.tensor.matmul(to, low_hot[q][:, c, at:at + P], part[:, c, :, :],
                                             start=(c == 0 and part is pick_hi), stop=False)
                    last = nc.tensor.matmul(to, high_hot[q][:, at:at + P], lower[:, :, :], start=False, stop=True)
                last.then_inc(s_pick, 1)

            def sum_span(hot, b, bank=None):
                bank = b % 2 if bank is None else bank
                for t in range(TILES):
                    last = nc.tensor.matmul(sums[bank][0:MC, 0:SPAN], mx[b][:, t, :], hot[:, t, :],
                                            start=(t == 0), stop=(t == TILES - 1))
                return last

            def scatter(n, b):
                pe.wait_ge(s_msg, n + 1)
                sum_span(onehot[b], b).then_inc(s_sum, 1)

            more = [pe.alloc_register(f"more{i}") for i in range(PAIR)]

            def load_pair(n, b, k):
                pe.reg_load(more, spans[0:1, bass.ds(((k - 1) * PAIRS + b // PAIR) * 2 * PAIR + PAIR, PAIR)])

            def scatter_further(b):
                with pe.If(as_count(pe, more[0]) + as_count(pe, more[1])):
                    for i in range(PAIR):
                        with pe.If(as_count(pe, more[i])):
                            with pe.Fori(0, as_count(pe, more[i])):
                                pe.reg_add(done, done, 1)
                                pe.wait_ge(s_ohx, pe.snap(done, min_val=1, max_val=NG * N_NODES))
                                sum_span(onehot_x, (b - PAIR + i) % BUFS, FURTHER).then_inc(s_sumx, 1)

            pe.wait_ge(s_w, 16 * 2)
            done = pe.alloc_register("further_done")
            pe.reg_mov(done, 0)
            hidden(0, 0, 0, 1)
            edge_matrices(0, 0, 0, 1)
            hidden(1, 1, 1, 1)
            pe.wait_ge(s_tables, 3)
            pick(0, 0, 0, 1)
            root_product()
            pick(1, 1, 1, 1)
            pe.wait_ge(s_rootc, 1)
            pe.wait_ge(s_ones, BUFS)

            def step(n, b, early, k):
                left = groups_left(n)
                if left >= 1:
                    edge_matrices(*ahead(n, b, early, k, 1))
                if b % PAIR == 0:
                    if early != 0:
                        scatter_further(b)
                    if early == 0:
                        pe.wait_ge(s_span, 16)
                    load_pair(n, b, k)
                if left >= 2:
                    hidden(*ahead(n, b, early, k, 2))
                    pick(*ahead(n, b, early, k, 2))
                scatter(n, b)

            loop_groups(pe, step)
            scatter_further(NG % BUFS)
            pe.wait_ge(s_all, 1)
            pe.wait_ge(s_close, 16)
            for i, part in enumerate(PARTS):
                for w in range(part.start, part.stop):
                    last = nc.tensor.matmul(closed[i][:, w - part.start, :], acc[:, w * P:(w + 1) * P], close[:, :],
                                            start=True, stop=True)
                last.then_inc(s_closed, 1)

        @block.vector
        def _(dve):
            chain = [0]

            def link(ins):
                chain[0] += 1
                ins.then_inc(s_v, 1)
                dve.wait_ge(s_v, chain[0])

            ALL = slice(0, WINS)

            def wide(row, part):
                return stat[:, row, part].rearrange("p (w a) -> p w a", a=1).to_broadcast([P, part.stop - part.start, C])

            def param(k, part):
                return row_params[:, k:k + 1, :].to_broadcast([P, part.stop - part.start, C])

            def norm(dst, src, part):
                link(nc.vector.tensor_reduce(stat[:, 0, part], src[:, part, :], axis=AX.X, op=ALU.add))
                link(nc.vector.scalar_tensor_tensor(dst[:, part, :], wide(0, part), -1.0 / C, src[:, part, :], ALU.mult, ALU.add))
                link(nc.vector.tensor_tensor(sq[:, part, :], dst[:, part, :], dst[:, part, :], ALU.mult))
                nc.vector.tensor_reduce(stat[:, 0, part], sq[:, part, :], axis=AX.X, op=ALU.add).then_inc(s_var, 1)

            def inverse(part, nth):
                dve.wait_ge(s_sd, nth)
                link(nc.vector.reciprocal(stat[:, 2, part], stat[:, 1, part]))

            nc.vector.memset(one[:, :], 1.0).then_inc(s_one, 1)
            nc.vector.memset(eps[:, :], EPS).then_inc(s_one, 1)
            nc.vector.memset(tiny[:, :], 1.0 / SCALE).then_inc(s_one, 1)
            for b in range(BUFS):
                nc.vector.memset(mx[b][:, :, C:C + 1], 1.0).then_inc(s_ones, 1)
            half = SUMS // 2
            nc.vector.memset(acc[:, 0:half], 0.0).then_inc(s_acc, 1)
            dve.wait_ge(s_x, 16)
            norm(cen, x_in, ALL)
            inverse(ALL, 1)
            nc.vector.scalar_tensor_tensor(xh[:, :, :], cen[:, :, :], 0.0, wide(2, ALL),
                                           ALU.max, ALU.mult).then_inc(s_xh, 1)
            dve.wait_ge(s_dst, 16)
            nc.vector.tensor_reduce(span_f[:, :, 0], dst_sb[:, :, :], axis=AX.X, op=ALU.min)
            link(nc.vector.tensor_reduce(span_f[:, :, 1], dst_sb[:, :, :], axis=AX.X, op=ALU.max))
            nc.vector.tensor_copy(span_w[:, 0, :], span_f[:, :, 0])
            link(nc.vector.scalar_tensor_tensor(span_f[:, :, 1], span_f[:, :, 1], float(N_NODES - 1), span_f[:, :, 0],
                                                ALU.min, ALU.subtract))
            link(nc.vector.tensor_scalar(span_f[:, :, 1], span_f[:, :, 1], 3, None, ALU.arith_shift_right))
            link(nc.vector.tensor_scalar(span_f[:, :, 1], span_f[:, :, 1], 205.0, None, ALU.mult))
            nc.vector.tensor_scalar(span_w[:, 1, :], span_f[:, :, 1], 10, None, ALU.arith_shift_right).then_inc(s_spanw, 1)

            dve.wait_ge(s_byte, 1)
            nc.vector.tensor_copy(minus[:, :], minus_i[:, :]).then_inc(s_minus, 1)
            dve.wait_ge(s_xh, 1)
            link(nc.vector.tensor_scalar(xh_scaled[:, :, :], xh[:, :, :], SCALE, None, ALU.mult))
            nc.vector.memset(pick_hi[:, :, :, :], 0.0)
            link(nc.vector.memset(pick_lo[:, :, :, :], 0.0))
            for c in range(CHUNKS):
                n_high = len(range(c, WINS, CHUNKS))
                of = xh_scaled[:, c:WINS:CHUNKS, :].rearrange("p w c -> p c w")
                link(nc.vector.tensor_copy(pick_hi[:, c, :, 0:n_high], of))
                nc.vector.tensor_tensor(pick_lo[:, c, :, 0:n_high], of, pick_hi[:, c, :, 0:n_high],
                                        ALU.subtract).then_inc(s_tables, 1)
            dve.wait_ge(s_low, 1)
            nc.vector.tensor_copy(lower[:, :, :], lower_f[:, :, :]).then_inc(s_tables, 1)
            full = (WINS * C) // P
            rest = WINS * C - full * P
            dve.wait_ge(s_xT, CH)
            nc.vector.tensor_copy(xT[:, 0:full, :], pT[:, 0:full * P].rearrange("p (k n) -> p k n", n=P))
            nc.vector.tensor_copy(xT[0:rest, full, :], pT[0:rest, full * P:(full + 1) * P]).then_inc(s_xTc, 1)
            nc.vector.memset(acc[:, half:SUMS], 0.0).then_inc(s_acc, 1)

            def select(n, b, early, k):
                dve.wait_ge(s_pick, n + 1)
                count = TILES - fetched(b)
                nc.vector.tensor_reduce(mx[b][:, fetched(b):TILES, C + 1:MC],
                                        picked[:, 0:count * C * HIGHS].rearrange("p (t c h) -> p t c h", c=C, h=HIGHS),
                                        axis=AX.X, op=ALU.max).then_inc(s_sel, 1)

            def span_hots(hot, b, node):
                span = node_i[:, bass.ds(node, SPAN)].rearrange("p (a j) -> p a j", a=1).to_broadcast([P, TILES, SPAN])
                dst = nodes[b // PAIR][:, 1, b % PAIR, :].rearrange("p (t a) -> p t a", a=1).to_broadcast([P, TILES, SPAN])
                return nc.vector.tensor_tensor(hot[:, :, :], span, dst, ALU.is_equal)

            node = [dve.alloc_register(f"node{i}") for i in range(BUFS)]
            more = [dve.alloc_register(f"more{i}") for i in range(BUFS)]
            start = dve.alloc_register("span_start")
            further = dve.alloc_register("further_done")
            dve.reg_mov(further, 0)

            def load_pair(n, b, early, k):
                dve.reg_load(node[b:b + PAIR] + more[b:b + PAIR],
                             spans[0:1, bass.ds(((k - 1) * PAIRS + b // PAIR) * 2 * PAIR, 2 * PAIR)])

            def one_hots(n, b, early, k):
                if b % PAIR == 0:
                    dve.wait_ge(s_nodes[b // PAIR], 16 * k)
                if early is None:
                    dve.wait_ge(s_sum, n - BUFS + 1)
                span_hots(onehot[b], b, as_node(dve, node[b])).then_inc(s_oh, 1)

            def fold(bank, at):
                return nc.vector.tensor_tensor(acc[:, bass.ds(at, SPAN)], sums[bank][0:MC, 0:SPAN],
                                               acc[:, bass.ds(at, SPAN)], ALU.add)

            def fold_first(n, b):
                dve.wait_ge(s_acc, n + 2)
                dve.wait_ge(s_sum, n + 1)
                fold(b % 2, as_node(dve, node[b])).then_inc(s_acc, 1)

            def fold_further(n, b):
                before = (b - 1) % BUFS
                with dve.If(as_count(dve, more[before]) + as_count(dve, more[b])):
                    for i in (before, b):
                        with dve.If(as_count(dve, more[i])):
                            dve.reg_mov(start, node[i])
                            with dve.Fori(0, as_count(dve, more[i])):
                                dve.reg_add(start, start, SPAN)
                                span_hots(onehot_x, i, as_node(dve, start)).then_inc(s_ohx, 1)
                                dve.reg_add(further, further, 1)
                                count = dve.snap(further, min_val=1, max_val=NG * N_NODES)
                                folded = dve.snap(n + 3)
                                dve.wait_ge(s_sumx, count)
                                dve.wait_ge(s_acc, folded)
                                fold(FURTHER, as_node(dve, start)).then_inc(s_accx, 1)
                                dve.wait_ge(s_accx, count)
                                dve.sem_inc(s_settled, 1)

            select(0, 0, 0, 1)
            dve.wait_ge(s_root, CH)
            dve.wait_ge(s_par, 16)
            nc.vector.tensor_tensor(root_part[:, :, :], pT[:, 0:WINS * C].rearrange("p (w c) -> p w c", c=C), param(0, ALL),
                                    ALU.add).then_inc(s_rootc, 1)

            def step(n, b, early, k):
                left = groups_left(n)
                dve.wait_ge(s_gath[b], 16 * fetched(b) * k)
                dve.wait_ge(s_sel, n + 1)
                dve.wait_ge(s_we, n + 1)
                xs = mx[b][:, :, C + 1:MC].rearrange("p t (a c) -> p t a c", a=1).to_broadcast([P, TILES, C, C])
                nc.vector.tensor_tensor(prod[b % 2][:, :, :, :], we[b % 2][:, :, :].rearrange("p t (o i) -> p t o i", i=C),
                                        xs, ALU.mult).then_inc(s_prod, 1)
                if left >= 1:
                    select(*ahead(n, b, early, k, 1))
                if early == 0:
                    dve.wait_ge(s_iota, 1)
                    dve.wait_ge(s_span, 16)
                    load_pair(0, 0, 0, 1)
                    one_hots(0, 0, 0, 1)
                if left >= 1:
                    one_hots(*ahead(n, b, early, k, 1))
                if early != 0:
                    fold_first(n - 1, (b - 1) % BUFS)
                dve.wait_ge(s_prod, n + 1)
                nc.vector.tensor_reduce(mx[b][:, :, 0:C], prod[b % 2][:, :, :, :], axis=AX.X, op=ALU.add).then_inc(s_msg, 1)
                if b % PAIR == 0:
                    if left >= PAIR:
                        load_pair(*ahead(n, b, early, k, PAIR))
                    if early != 0:
                        fold_further(n - 1, (b - 1) % BUFS)

            loop_groups(dve, step)
            fold_first(NG - 1, (NG - 1) % BUFS)
            fold_further(NG - 1, (NG - 1) % BUFS)
            dve.drain().then_inc(s_all, 1)
            link(nc.vector.tensor_tensor(xh_b[:, :, :], xh[:, :, :], param(2, ALL), ALU.add))
            for i, part in enumerate(PARTS):
                dve.wait_ge(s_closed, 1 + i)
                link(nc.vector.tensor_scalar(stat[:, 0, part], closed[i][:, :, C], 1.0, None, ALU.max))
                link(nc.vector.reciprocal(stat[:, 2, part], stat[:, 0, part]))
                link(nc.vector.tensor_tensor(cen[:, part, :], closed[i][:, :, 0:C], wide(2, part), ALU.mult))
                link(nc.vector.tensor_tensor(root_part[:, part, :], cen[:, part, :], root_part[:, part, :], ALU.add))
                norm(cen, root_part, part)
            for i, part in enumerate(PARTS):
                inverse(part, 2 + i)
                link(nc.vector.tensor_tensor(cen[:, part, :], cen[:, part, :], wide(2, part), ALU.mult))
                link(nc.vector.tensor_tensor(cen[:, part, :], cen[:, part, :], param(1, part), ALU.mult))
                nc.vector.tensor_tensor(cen[:, part, :], cen[:, part, :], xh_b[:, part, :], ALU.add).then_inc(s_pre, 1)
            for i, part in enumerate(PARTS):
                dve.wait_ge(s_act, 1 + i)
                nc.vector.tensor_tensor(cen[:, part, :], sq[:, part, :], x_in[:, part, :], ALU.add).then_inc(s_fin, 1)


def kernel(x, src, dst, edge_attr_8, L0_gnn_W1, L0_gnn_b1, L0_gnn_W2, L0_gnn_b2, L0_gnn_root, L0_gnn_bias,
           L0_gnn_ln_w, L0_gnn_ln_b):
    import numpy as np
    import concourse.bacc as bacc
    from concourse.bass_utils import run_bass_kernel_spmd as run

    pad = NG * GE - N_EDGES
    src_p = np.pad(np.asarray(src), (0, pad)).reshape(NG, TILES, P)
    dst_p = np.pad(np.asarray(dst), (0, pad), constant_values=PAD_DST).reshape(NG, TILES, P)
    ea_p = np.pad(np.asarray(edge_attr_8), ((0, pad), (0, 0))).reshape(NG // PAIR, PAIR, TILES // HALVES, HALVES, P, ED)
    w1, b1 = np.asarray(L0_gnn_W1), np.asarray(L0_gnn_b1)
    w2 = np.asarray(L0_gnn_W2).reshape(HID, C, C).transpose(0, 2, 1).reshape(HID, C * C)
    w1_rows = np.zeros((P, P), w1.dtype)
    w2_rows = np.zeros((P, HALVES * C * C), w2.dtype)
    for h in range(HALVES):
        w1_rows[h * ED:(h + 1) * ED, h * HID:(h + 1) * HID] = w1
        w1_rows[HALVES * ED, h * HID:(h + 1) * HID] = b1
        w2_rows[h * HID:(h + 1) * HID, h * C * C:(h + 1) * C * C] = w2
    root_rows = np.zeros((P, P), np.asarray(L0_gnn_root).dtype)
    for d in range(0, P, C):
        root_rows[d:d + C, d:d + C] = np.asarray(L0_gnn_root)
    close_rows = np.eye(MC, C + 1, dtype=np.asarray(L0_gnn_b2).dtype)
    close_rows[C + 1:, 0:C] = np.asarray(L0_gnn_b2).reshape(C, C)
    edge_t = np.empty((NG // PAIR, HALVES * ED + 1, PAIR, HE), ea_p.dtype)
    edge_t[:, :-1] = ea_p.transpose(0, 3, 5, 1, 2, 4).reshape(NG // PAIR, HALVES * ED, PAIR, HE)
    edge_t[:, -1] = 1
    all_src = np.pad(src_p, ((0, -NG % len(PICKS)), (0, 0), (0, 0))).reshape(-1, len(PICKS), TILES, P)
    arrays = {
        "x": np.pad(np.asarray(x), ((0, WINS * P - N_NODES), (0, 0))),
        "edge_t": edge_t,
        "edge_nodes": np.stack([src_p, dst_p]).reshape(2, NG // PAIR, PAIR, TILES, P).transpose(1, 4, 0, 2, 3),
        "pick_src": np.concatenate([all_src[:, i, TILES - p:].reshape(-1, p * P)
                                    for i, p in enumerate(PICKS)], axis=1),
        "dst_rows": dst_p.reshape(NG, GE),
        "w1_rows": w1_rows,
        "w2_rows": w2_rows,
        "root_rows": root_rows,
        "close_rows": close_rows,
        "rows": np.broadcast_to(np.stack([np.asarray(L0_gnn_bias), np.asarray(L0_gnn_ln_w), np.asarray(L0_gnn_ln_b)]),
                                (P, 3, C)),
    }
    arrays = {k: np.ascontiguousarray(v) for k, v in arrays.items()}
    nc = bacc.Bacc("TRN2", target_bir_lowering=False, num_devices=1)
    aps = {k: nc.dram_tensor(k, v.shape, mybir.dt.from_np(v.dtype), kind="ExternalInput").ap() for k, v in arrays.items()}
    x_table = nc.dram_tensor("x_table", (WINS * P, C), mybir.dt.float32, kind="Internal").ap()
    span_table = nc.dram_tensor("span_table", (NG * 2,), mybir.dt.int32, kind="Internal").ap()
    out = nc.dram_tensor("out", (N_NODES, C), mybir.dt.float32, kind="ExternalOutput").ap()
    gnn_layer(nc, x_table=x_table, span_table=span_table, out=out, **aps)
    return run(nc, [arrays], core_ids=[0]).results[0]["out"]
```
